# Optimizing a Trainium2 kernel written in Bass

```python
import numpy as np
import jax
import jax.numpy as jnp

def _softmax(x, axis=-1):
    return jax.nn.softmax(x, axis=axis)
def _gelu(x):
    return jax.nn.gelu(x, approximate=True)
def _silu(x):
    return jax.nn.silu(x)
def _sigmoid(x):
    return jax.nn.sigmoid(x)
def _layernorm(x, axis=-1, eps=1e-5):
    m = jnp.mean(x, axis=axis, keepdims=True)
    v = jnp.var(x, axis=axis, keepdims=True)
    return (x - m) / jnp.sqrt(v + eps)
def _scatter_add(tgt, idx, src, axis=0):
    return tgt.at[idx].add(src)
def _segment_sum(src, seg, n):
    return jax.ops.segment_sum(src, seg, n)

kernel_name = 'mk_conv_seq_d1_conv_nhwc768_a81cee'

def setup_inputs(seed: int = 0):
    np.random.seed(seed)
    _w = jnp.asarray
    def _rec_inputs():
        import jax
        import jax.numpy as jnp
        _gk = jax.random.key(seed)
        x = -4.65e-05 + 0.9999 * jax.random.normal(jax.random.fold_in(_gk, 1), (4, 128, 128, 768), jnp.float32)
        return x
    x = _rec_inputs()
    def _L0_conv_setup():
        import jax, jax.numpy as jnp
        import numpy as np
        B, H, W, C = (4, 128, 128, 768)
        NUM_BLOCKS = 8
        BLOCK = C // NUM_BLOCKS
        HSF = 1
        SCALE = 0.02
        LAMBD = 0.01
        HARD_FRAC = 1.0

        def softshrink(v, lambd):
            return jnp.where(v > lambd, v - lambd, jnp.where(v < -lambd, v + lambd, 0.0))
        key = jax.random.key(seed)
        ks = jax.random.split(key, 5)
        return {'x': jax.random.normal(ks[0], (B, H, W, C), dtype=jnp.float32), 'w1': SCALE * jax.random.normal(ks[1], (2, NUM_BLOCKS, BLOCK, BLOCK * HSF), dtype=jnp.float32), 'b1': SCALE * jax.random.normal(ks[2], (2, NUM_BLOCKS, BLOCK * HSF), dtype=jnp.float32), 'w2': SCALE * jax.random.normal(ks[3], (2, NUM_BLOCKS, BLOCK * HSF, BLOCK), dtype=jnp.float32), 'b2': SCALE * jax.random.normal(ks[4], (2, NUM_BLOCKS, BLOCK), dtype=jnp.float32)}
    _L0_conv_all = _L0_conv_setup()
    _L0_conv_in = {k: v for k, v in _L0_conv_all.items() if k in ('w1', 'b1', 'w2', 'b2', )}
    del _L0_conv_all

    return {
        "x": x,
        "L0_conv_w1": _L0_conv_in["w1"],
        "L0_conv_b1": _L0_conv_in["b1"],
        "L0_conv_w2": _L0_conv_in["w2"],
        "L0_conv_b2": _L0_conv_in["b2"],
    }

def reference(x, L0_conv_w1, L0_conv_b1, L0_conv_w2, L0_conv_b2):
    import jax
    import jax.numpy as jnp
    def _L0_conv_ref(x, w1, b1, w2, b2):
        import jax, jax.numpy as jnp
        import numpy as np
        B, H, W, C = (4, 128, 128, 768)
        NUM_BLOCKS = 8
        BLOCK = C // NUM_BLOCKS
        HSF = 1
        SCALE = 0.02
        LAMBD = 0.01
        HARD_FRAC = 1.0

        def softshrink(v, lambd):
            return jnp.where(v > lambd, v - lambd, jnp.where(v < -lambd, v + lambd, 0.0))
        bias = x
        dtype = x.dtype
        xf = jnp.fft.rfft2(x.astype(jnp.float32), axes=(1, 2), norm='ortho')
        b, h, wf, c = xf.shape
        xf = xf.reshape(b, h, wf, NUM_BLOCKS, BLOCK)
        total_modes = H * W // 2 + 1
        kept = min(int(total_modes * HARD_FRAC), wf)
        xr = jnp.real(xf[:, :, :kept])
        xi = jnp.imag(xf[:, :, :kept])
        o1r = jax.nn.relu(jnp.einsum('bhwni,nio->bhwno', xr, w1[0]) - jnp.einsum('bhwni,nio->bhwno', xi, w1[1]) + b1[0])
        o1i = jax.nn.relu(jnp.einsum('bhwni,nio->bhwno', xi, w1[0]) + jnp.einsum('bhwni,nio->bhwno', xr, w1[1]) + b1[1])
        o2r = jnp.einsum('bhwno,noi->bhwni', o1r, w2[0]) - jnp.einsum('bhwno,noi->bhwni', o1i, w2[1]) + b2[0]
        o2i = jnp.einsum('bhwno,noi->bhwni', o1i, w2[0]) + jnp.einsum('bhwno,noi->bhwni', o1r, w2[1]) + b2[1]
        o2r = softshrink(o2r, LAMBD)
        o2i = softshrink(o2i, LAMBD)
        if kept < wf:
            pad = [(0, 0), (0, 0), (0, wf - kept), (0, 0), (0, 0)]
            o2r = jnp.pad(o2r, pad)
            o2i = jnp.pad(o2i, pad)
        xc = (o2r + 1j * o2i).reshape(b, h, wf, c)
        out = jnp.fft.irfft2(xc, s=(H, W), axes=(1, 2), norm='ortho').astype(dtype)
        return out + bias

    def _gn(v, G=32, eps=1e-5):
        B_, H_, W_, C_ = v.shape
        g = v.reshape(B_, H_, W_, G, C_ // G)
        m = jnp.mean(g, axis=(1, 2, 4), keepdims=True)
        s = jnp.var(g, axis=(1, 2, 4), keepdims=True)
        return ((g - m) / jnp.sqrt(s + eps)).reshape(v.shape)

    def _ln_c(v, eps=1e-6):
        m = jnp.mean(v, axis=-1, keepdims=True)
        s = jnp.var(v, axis=-1, keepdims=True)
        return (v - m) / jnp.sqrt(s + eps)

    def _ln_t(v, eps=1e-5):
        m = jnp.mean(v, axis=-1, keepdims=True)
        s = jnp.var(v, axis=-1, keepdims=True)
        return (v - m) / jnp.sqrt(s + eps)

    def _to_tokens(v):
        B_, H_, W_, C_ = v.shape
        return v.reshape(B_, H_ * W_, C_)
    def _from_tokens(t, like):
        return t.reshape(like.shape)

    x = _L0_conv_ref(x, L0_conv_w1, L0_conv_b1, L0_conv_w2, L0_conv_b2)
    return x


_drawn_inputs = setup_inputs


def setup_inputs(seed=0):
    import zlib

    import numpy as np

    out = dict(_drawn_inputs(seed))
    spreads = {}
    factors = {'L0_conv_b1': 8.0}
    for name, (base, spread) in spreads.items():
        noise = np.random.default_rng([zlib.crc32(name.encode()), seed]).standard_normal(out[name].shape)
        drawn = base * np.exp(spread * noise) if base else spread * noise
        out[name] = jnp.asarray(drawn.astype(out[name].dtype))
    for name, factor in factors.items():
        out[name] = (out[name] * factor).astype(out[name].dtype)
    return out
```

```python
from contextlib import ExitStack

import concourse.bass as bass
from concourse import mybir

ACT = mybir.ActivationFunctionType
ALU = mybir.AluOpType
F32 = mybir.dt.float32
F32R = mybir.dt.float32r

B, H, W, C = 4, 128, 128, 768
NB = 8
CB = C // NB
LAMBD = 0.01
HC = H // 2 + 1
HS = H // 2 - 1
KW = W // 2 + 1
PAIRS = 2
STEPS = B * NB // PAIRS

CG = 4
NG = CB // CG
KU = 3
NU = 1 + (KW - 2) // KU
HG = 5
NF = HC // HG
STORE_AFTER = (3, 6, 9, 12)
LOADS = 4
STORES = 2 * len(STORE_AFTER)
WEIGHT_DMAS = 5

COLS = {}
_at = 0
for _name, _n in (("fwd_w", W), ("fwd_h", 2 * HC), ("inv_h", H), ("inv_w_even", W), ("inv_w_odd", W),
                  ("merge_even", H), ("merge_odd", H)):
    COLS[_name] = (_at, _at + _n)
    _at += _n
TABLE = _at


def transform_table():
    import numpy as np

    def cos(a, b):
        k = np.outer(a, b) % 128
        v = np.cos(2 * np.pi * k / 128)
        v[(k == 32) | (k == 96)] = 0.0
        return v

    def sin(a, b):
        return cos(a, b) * 0 + np.where(np.outer(a, b) % 64 == 0, 0.0, np.sin(2 * np.pi * (np.outer(a, b) % 128) / 128))

    n = np.arange(128)
    kw = np.arange(1, 64)
    kh = np.concatenate([np.arange(0, 65), -np.arange(1, 64)])
    fwd_w = np.zeros((128, 128))
    fwd_w[:, 0] = 1.0
    fwd_w[:, 1] = 1.0 - 2.0 * (n % 2)
    fwd_w[:, 2::2] = cos(n, kw)
    fwd_w[:, 3::2] = -sin(n, kw)
    half = np.arange(0, 65)
    fwd_h = np.concatenate([cos(n, half), sin(n, half)], 1)
    inv_h = np.concatenate([cos(kh, half), sin(kh, kw)], 1)
    inv_even = np.zeros((128, 128))
    inv_even[0] = 1.0
    inv_even[1] = 1.0 - 2.0 * (n % 2)
    inv_even[2::2] = 2.0 * cos(kw, n)
    inv_even[3::2] = -2.0 * sin(kw, n)
    inv_odd = np.zeros((128, 128))
    inv_odd[0] = -1.0
    inv_odd[1] = -(1.0 - 2.0 * (n % 2))
    inv_odd[2::2] = -2.0 * sin(kw, n)
    inv_odd[3::2] = -2.0 * cos(kw, n)
    flip = (kh[:, None] == -kh[None, :]) | ((kh[:, None] + kh[None, :]) == 128)
    eye = np.eye(128)
    merge_even = (eye + flip) / 2
    merge_odd = (eye - flip) / 2
    return np.concatenate([fwd_w / 128, fwd_h, inv_h, inv_even / 128, inv_odd / 128,
                           merge_even, merge_odd], 1).astype(np.float32)


def build(nc, x, w1, b1, w2, b2, table, out):
    with ExitStack() as ctx:
        def sb(name, shape, dt=F32):
            return ctx.enter_context(nc.sbuf_tensor(name, shape, dt))

        def sem(name):
            return ctx.enter_context(nc.semaphore(name))

        tab = sb("tab", [128, TABLE])
        xs = [sb(f"x{p}", [W, H, CB]) for p in range(PAIRS)]
        ydg = sb("ydg", [128, 128, CB])
        w1s = sb("w1s", [CB, 2, CB])
        w1n = sb("w1n", [CB, CB])
        b1s = sb("b1s", [CB, 2])
        w2r = sb("w2r", [CB + 1, 2, CB])
        w2i = sb("w2i", [CB, 2, CB])
        pcopy = [sb(f"pcopy{j}", [CB, KU, 2 * HC]) for j in range(2)]
        z = [sb(f"z{j}", [CB, 2, KU, H]) for j in range(2)]
        hid = [sb(f"hid{j}", [CB + 1, 2, KU, H]) for j in range(2)]
        clamped = [sb(f"clamped{j}", [128, KU, 2 * CB]) for j in range(2)]
        edge = sb("edge", [128, 2, 2, CB])
        vcopy = [sb(f"vcopy{j}", [W, HG, CB]) for j in range(3)]
        ps = ctx.enter_context(nc.psum_tensor("ps", [128, 8, 512], F32))

        table_loaded = sem("table_loaded")
        ones_set = sem("ones_set")
        x_loaded = [sem(f"x_loaded{p}") for p in range(PAIRS)]
        stored = [sem(f"stored{p}") for p in range(PAIRS)]
        weights_loaded = sem("weights_loaded")
        weights_ready = sem("weights_ready")
        line_done = sem("line_done")
        line_act = sem("line_act")
        line_dve = sem("line_dve")
        p_done = sem("p_done")
        q_done = sem("q_done")
        p_copied = sem("p_copied")
        z_ready = sem("z_ready")
        mix1r_done = sem("mix1r_done")
        mix1i_done = sem("mix1i_done")
        hid_ready = sem("hid_ready")
        mix2_done = sem("mix2_done")
        clamp_done = sem("clamp_done")
        shrunk = sem("shrunk")
        merge_done = sem("merge_done")
        merged = sem("merged")
        u_done = sem("u_done")
        v_done = sem("v_done")
        v_copied = sem("v_copied")
        plus_ready = sem("plus_ready")
        minus_ready = sem("minus_ready")
        y_ready = sem("y_ready")

        def mat(name):
            a, b = COLS[name]
            return tab[:, a:b]

        P_BANK, Q_BANK, O_BANK, M_BANK, E_BANK = 0, 1, 2, 4, 7

        def line_bank(stage, g):
            return (g + 2) % 8 if stage == 0 else g % 8

        def line_psum(bank):
            return ps[:, bank, :].rearrange("p (c k) -> p k c", c=CG)

        def odd_rows(g):
            return max(HG * g, 1), min(HG * g + HG, H // 2)

        def mirror(t, a, b):
            return t[:, H - a:H - b:-1, :]

        with nc.Block() as block:

            @block.sync
            def _(sp):
                sp.dma_start(tab[:], table).then_inc(table_loaded, 16)

                def load_x(n, b, p):
                    src = x[bass.ds(b, 1), :, :, bass.ds(n * CB, CB)].rearrange("o h w c -> (o w) h c")
                    for i in range(LOADS):
                        rows = slice(i * H // LOADS, (i + 1) * H // LOADS)
                        sp.dma_start(xs[p][:, rows, :], src[:, rows, :]).then_inc(x_loaded[p], 16)

                def load_weights(n):
                    one = bass.ds(n, 1)
                    sp.dma_start(w1s[:], w1[:, one].rearrange("r o i j -> (o i) r j")).then_inc(weights_loaded, 16)
                    sp.dma_start(b1s[:], b1[:, one].rearrange("r o (i z) -> (o i) r z", z=1)).then_inc(weights_loaded, 16)
                    sp.dma_start(w2r[0:CB], w2[:, one].rearrange("r o i j -> (o i) r j")).then_inc(weights_loaded, 16)
                    sp.dma_start(w2r[CB:CB + 1], b2[:, one].rearrange("r o j -> o r j")).then_inc(weights_loaded, 16)
                    sp.dma_start(w2i[:, 1, :], w2[0:1, one].rearrange("r o i j -> (r o i) j")).then_inc(weights_loaded, 16)

                with nc.allow_non_contiguous_dma(reason="biases, one element per partition"):
                    load_x(0, 0, 0)
                    load_weights(0)
                    load_x(0, 1, 1)
                    def step(t, last):
                        for p in range(PAIRS):
                            q = t * PAIRS + p
                            if p == PAIRS - 1 and not last:
                                sp.wait_ge(mix2_done, NU * q + NU)
                                load_weights((q + 1) // B)
                            b = q % B
                            dst = out[bass.ds(b, 1), :, :, bass.ds(q // B * CB, CB)].rearrange("o h w c -> (o w) h c")
                            a = 0
                            for g in STORE_AFTER:
                                e = HG * (g + 1)
                                sp.wait_ge(y_ready, NF * q + NF + g + 1)
                                sp.dma_start(dst[:, a:e, :], xs[p][:, a:e, :]).then_inc(stored[p], 16)
                                lo, hi = H - min(e, H // 2) + 1, H - max(a, 1) + 1
                                sp.dma_start(dst[:, lo:hi, :], xs[p][:, lo:hi, :]).then_inc(stored[p], 16)
                                a = e
                            sp.wait_ge(stored[p], (t + 1) * 16 * STORES)
                            if not last:
                                load_x((q + PAIRS) // B, (q + PAIRS) % B, p)

                    with sp.Fori(0, STEPS - 1) as t:
                        step(t, False)
                    step(STEPS - 1, True)

            @block.tensor
            def _(pe):
                def lines(q, t, p, stage):
                    src = xs[p] if stage == 0 else ydg
                    rhs = mat("fwd_w") if stage == 0 else mat("inv_h")
                    for g in range(NG):
                        bank = line_bank(stage, g)
                        if g >= 8:
                            freed = line_dve if g % 2 else line_act
                            pe.wait_ge(freed, NG * q + stage * NG // 2 + (g - 8) // 2 + 1)
                        elif stage == 0 and g % 2 == 0:
                            pe.wait_ge(y_ready, NF * q + NF - 4 + g // 2 + 1)
                        for j in range(CG):
                            mm = pe.matmul(ps[:, bank, j * 128:(j + 1) * 128], src[:, :, g * CG + j], rhs,
                                           start=True, stop=True)
                        mm.then_inc(line_done, 1)

                def lines_moved(q, stage):
                    n = NG * q + (stage + 1) * NG // 2
                    pe.wait_ge(line_act, n)
                    pe.wait_ge(line_dve, n)

                def fwd_h(q, v):
                    if v:
                        pe.wait_ge(z_ready, NU * q + v)
                    for part in range(2 if v else 1):
                        for k in range(KU if v else 2):
                            idx = 2 * (1 + KU * (v - 1) + k) + part if v else k
                            mm = pe.matmul(ps[0:CB, part, k * 2 * HC:(k + 1) * 2 * HC], ydg[:, idx, :], mat("fwd_h"),
                                           start=True, stop=True)
                        mm.then_inc((p_done, q_done)[part], 1)

                def mix1(q, v):
                    pe.wait_ge(z_ready, NU * q + v + 1)
                    if v:
                        pe.wait_ge(hid_ready, NU * q + v)
                    n = (KU if v else 2)
                    zr, zi = z[v % 2][:, 0, 0:n, :], z[v % 2][:, 1, 0:n, :]
                    o = [ps[0:CB, O_BANK + i, 0:n * H] for i in range(2)]
                    pe.matmul(o[0], w1s[:, 0, :], zr, start=True, stop=False)
                    pe.matmul(o[0], w1n[:], zi, start=False, stop=True).then_inc(mix1r_done, 1)
                    pe.matmul(o[1], w1s[:, 0, :], zi, start=True, stop=False)
                    pe.matmul(o[1], w1s[:, 1, :], zr, start=False, stop=True).then_inc(mix1i_done, 1)

                def mix2(q, v):
                    pe.wait_ge(hid_ready, NU * q + v + 1)
                    if v:
                        pe.wait_ge(shrunk, NU * q + v)
                    for k in range(KU if v else 2):
                        o = ps[:, M_BANK + k, 0:2 * CB]
                        pe.matmul(o, hid[v % 2][:, 0, k, :], w2r[:].rearrange("p r c -> p (r c)"),
                                  start=True, stop=False)
                        mm = pe.matmul(o, hid[v % 2][0:CB, 1, k, :], w2i[:].rearrange("p r c -> p (r c)"),
                                       start=False, stop=True)
                    mm.then_inc(mix2_done, 1)

                def merge(q):
                    pe.wait_ge(shrunk, NU * q + 1)
                    o = ps[:, E_BANK, 0:2 * CB].rearrange("p (k c) -> p k c", k=2)
                    pe.matmul(o, mat("merge_even"), edge[:, :, 0, :], start=True, stop=False)
                    pe.matmul(o, mat("merge_odd"), edge[:, :, 1, :], start=False, stop=True).then_inc(merge_done, 1)

                def rows(q, g):
                    bank = 2 * (g % 4)
                    if g >= 4:
                        pe.wait_ge(y_ready, NF * q + NF + g - 3)
                    a, b = odd_rows(g)
                    pe.matmul(ps[:, bank + 1, 0:(b - a) * CB], mat("inv_w_odd"),
                              ydg[:, HC + a - 1:HC + b - 1, :].rearrange("p h c -> p (h c)"),
                              start=True, stop=True).then_inc(v_done, 1)
                    pe.matmul(ps[:, bank, 0:HG * CB], mat("inv_w_even"),
                              ydg[:, HG * g:HG * g + HG, :].rearrange("p h c -> p (h c)"),
                              start=True, stop=True).then_inc(u_done, 1)

                pe.wait_ge(table_loaded, 16)
                pe.wait_ge(ones_set, 2)
                with pe.Fori(0, STEPS) as t:
                    for p in range(PAIRS):
                        q = t * PAIRS + p
                        pe.wait_ge(x_loaded[p], (t + 1) * 16 * LOADS)
                        lines(q, t, p, 0)
                        lines_moved(q, 0)
                        if p == 0:
                            pe.wait_ge(weights_ready, t + 1)
                        for v in range(NU + 2):
                            if v < NU:
                                fwd_h(q, v)
                            if 1 <= v <= NU:
                                mix1(q, v - 1)
                            if v >= 2:
                                mix2(q, v - 2)
                            if v == 4:
                                merge(q)
                        pe.wait_ge(shrunk, NU * q + NU)
                        pe.wait_ge(merged, q + 1)
                        lines(q, t, p, 1)
                        lines_moved(q, 1)
                        for g in range(NF):
                            rows(q, g)

            @block.scalar
            def _(act):
                def lines(q, stage):
                    for g in range(0, NG, 2):
                        act.wait_ge(line_done, 2 * NG * q + stage * NG + g + 1)
                        act.copy(ydg[:, :, g * CG:(g + 1) * CG], line_psum(line_bank(stage, g))).then_inc(line_act, 1)

                act.wait_ge(ones_set, 2)
                with act.Fori(0, STEPS) as t:
                    for p in range(PAIRS):
                        q = t * PAIRS + p
                        lines(q, 0)
                        if p == 0:
                            act.wait_ge(weights_loaded, (t + 1) * 16 * WEIGHT_DMAS)
                            act.mul(w1n[:], w1s[:, 1, :], -1.0)
                            act.mul(w2i[:, 0, :], w2r[0:CB, 1, :], -1.0).then_inc(weights_ready, 1)
                        for v in range(NU + 1):
                            if 1 <= v < NU:
                                act.wait_ge(p_done, NU * q + v + 1)
                                if v >= 2:
                                    act.wait_ge(z_ready, NU * q + v - 1)
                                act.copy(pcopy[v % 2][:].rearrange("p k n -> p (k n)"),
                                         ps[0:CB, P_BANK, 0:KU * 2 * HC]).then_inc(p_copied, 1)
                            if v >= 1:
                                u = v - 1
                                n = (KU if u else 2) * H
                                if u >= 2:
                                    act.wait_ge(mix2_done, NU * q + u - 1)
                                for i in range(2):
                                    act.wait_ge((mix1r_done, mix1i_done)[i], NU * q + u + 1)
                                    ins = act.activation(hid[u % 2][0:CB, i].rearrange("p k n -> p (k n)")[:, 0:n],
                                                         ps[0:CB, O_BANK + i, 0:n], ACT.Relu, bias=b1s[:, i:i + 1])
                                ins.then_inc(hid_ready, 1)
                            if v == 5:
                                act.wait_ge(merge_done, q + 1)
                                act.copy(ydg[:, 0:2, :].rearrange("p k c -> p (k c)"),
                                         ps[:, E_BANK, 0:2 * CB]).then_inc(merged, 1)
                        lines(q, 1)
                        for g in range(NF):
                            act.wait_ge(v_done, NF * q + g + 1)
                            if g >= 3:
                                act.wait_ge(y_ready, NF * q + NF + g - 2)
                            a, b = odd_rows(g)
                            act.copy(vcopy[g % 3][:, 0:b - a, :].rearrange("p h c -> p (h c)"),
                                     ps[:, 2 * (g % 4) + 1, 0:(b - a) * CB]).then_inc(v_copied, 1)

            @block.vector
            def _(dve):
                def lines(q, stage):
                    for g in range(1, NG, 2):
                        dve.wait_ge(line_done, 2 * NG * q + stage * NG + g + 1)
                        dve.tensor_copy(ydg[:, :, g * CG:(g + 1) * CG],
                                        line_psum(line_bank(stage, g))).then_inc(line_dve, 1)

                def modes(q, v):
                    zr, zi = z[v % 2][:, 0], z[v % 2][:, 1]
                    if v >= 2:
                        dve.wait_ge(mix1i_done, NU * q + v - 1)
                    if v == 0:
                        dve.wait_ge(p_done, NU * q + 1)
                        pp = ps[0:CB, P_BANK, 0:2 * 2 * HC].rearrange("p (k n) -> p k n", k=2)
                        dve.tensor_copy(zr[:, 0:2, 0:HC], pp[:, :, 0:HC])
                        dve.tensor_copy(zr[:, 0:2, HC:H], pp[:, :, 1:HC - 1])
                        dve.tensor_scalar(zi[:, 0:2, 0:HC], pp[:, :, HC:2 * HC], -1.0, None, ALU.mult)
                        dve.tensor_copy(zi[:, 0:2, HC:H], pp[:, :, HC + 1:2 * HC - 1]).then_inc(z_ready, 1)
                        return
                    pc = pcopy[v % 2]
                    pq = ps[0:CB, Q_BANK, 0:KU * 2 * HC].rearrange("p (k n) -> p k n", k=KU)
                    dve.wait_ge(p_copied, (NU - 1) * q + v)
                    dve.wait_ge(q_done, (NU - 1) * q + v)
                    dve.tensor_tensor(zr[:, :, 0:HC], pq[:, :, HC:2 * HC], pc[:, :, 0:HC], ALU.add)
                    dve.tensor_tensor(zr[:, :, HC:H], pc[:, :, 1:HC - 1], pq[:, :, HC + 1:2 * HC - 1], ALU.subtract)
                    dve.tensor_tensor(zi[:, :, 0:HC], pq[:, :, 0:HC], pc[:, :, HC:2 * HC], ALU.subtract)
                    dve.tensor_tensor(zi[:, :, HC:H], pq[:, :, 1:HC - 1], pc[:, :, HC + 1:2 * HC - 1],
                                      ALU.add).then_inc(z_ready, 1)

                def shrink(q, v):
                    n = KU if v else 2
                    d = ps[:, M_BANK:M_BANK + n, 0:2 * CB]
                    c = clamped[v % 2][:, 0:n, :]
                    if v:
                        lo = 2 * (1 + KU * (v - 1))
                        dst = ydg[:, lo:lo + 2 * KU, :].rearrange("p (k r) c -> p k (r c)", r=2)
                    else:
                        dst = edge[:].rearrange("p k r c -> p k (r c)")
                    dve.wait_ge(mix2_done, NU * q + v + 1)
                    if v >= 2:
                        dve.wait_ge(shrunk, NU * q + v - 1)
                    dve.tensor_scalar(c, d, LAMBD, -LAMBD, ALU.min, ALU.max).then_inc(clamp_done, 1)
                    dve.wait_ge(clamp_done, NU * q + v + 1)
                    dve.tensor_tensor(dst, d, c, ALU.subtract).then_inc(shrunk, 1)

                def finish(q, p, g):
                    a, b = odd_rows(g)
                    xm = mirror(xs[p], a, b)
                    u = ps[:, 2 * (g % 4), 0:HG * CB].rearrange("p (h c) -> p h c", c=CB)
                    dve.wait_ge(v_copied, NF * q + g + 1)
                    dve.tensor_tensor(xm, xm, vcopy[g % 3][:, 0:b - a, :], ALU.subtract).then_inc(minus_ready, 1)
                    xp = xs[p][:, HG * g:HG * g + HG, :]
                    dve.wait_ge(u_done, NF * q + g + 1)
                    dve.wait_ge(plus_ready, NF * q + g + 1)
                    dve.tensor_tensor(xp, u, xp, ALU.add)
                    dve.wait_ge(minus_ready, NF * q + g + 1)
                    dve.tensor_tensor(xm, u[:, a - HG * g:b - HG * g, :], xm, ALU.add).then_inc(y_ready, 1)

                dve.memset(hid[0][CB:CB + 1, 0], 1.0).then_inc(ones_set, 1)
                dve.memset(hid[1][CB:CB + 1, 0], 1.0).then_inc(ones_set, 1)
                dve.memset(clamped[0][0:1, 0, 0:1], 0.0).then_inc(y_ready, NF)
                dve.wait_ge(y_ready, NF)
                with dve.Fori(0, STEPS) as t:
                    for p in range(PAIRS):
                        q = t * PAIRS + p
                        lines(q, 0)
                        for v in range(NU + 2):
                            if v < NU:
                                modes(q, v)
                            if v >= 2:
                                shrink(q, v - 2)
                        lines(q, 1)
                        for g in range(NF):
                            finish(q, p, g)

            @block.gpsimd
            def _(pool):
                with pool.Fori(0, STEPS) as t:
                    for p in range(PAIRS):
                        q = t * PAIRS + p
                        for g in range(NF):
                            a, b = odd_rows(g)
                            xp = xs[p][:, a:b, :]
                            pool.wait_ge(v_copied, NF * q + g + 1)
                            pool.tensor_tensor(xp, xp, vcopy[g % 3][:, 0:b - a, :], ALU.add).then_inc(plus_ready, 1)


def kernel(x, L0_conv_w1, L0_conv_b1, L0_conv_w2, L0_conv_b2):
    import numpy as np
    import concourse.bacc as bacc
    from concourse.bass_utils import run_bass_kernel_spmd

    nc = bacc.Bacc("TRN2", target_bir_lowering=False, num_devices=1)
    arrays = {"x": x, "w1": L0_conv_w1, "b1": L0_conv_b1, "w2": L0_conv_w2, "b2": L0_conv_b2,
              "table": transform_table()}
    arrays = {name: np.ascontiguousarray(a) for name, a in arrays.items()}
    args = [nc.dram_tensor(f"in_{name}", a.shape, mybir.dt.from_np(a.dtype), kind="ExternalInput").ap()
            for name, a in arrays.items()]
    out = nc.dram_tensor("out", (B, H, W, C), F32, kind="ExternalOutput").ap()
    build(nc, *args, out)
    r = run_bass_kernel_spmd(nc, [{f"in_{name}": a for name, a in arrays.items()}], core_ids=[0])
    return r.results[0]["out"]
```

```python
from contextlib import ExitStack

import concourse.bass as bass
from concourse import mybir

ACT = mybir.ActivationFunctionType
ALU = mybir.AluOpType
F32 = mybir.dt.float32
F32R = mybir.dt.float32r

B, H, W, C = 4, 128, 128, 768
NB = 8
CB = C // NB
LAMBD = 0.01
HC = H // 2 + 1
HS = H // 2 - 1
KW = W // 2 + 1
PAIRS = 2
STEPS = B * NB // PAIRS

CG = 4
NG = CB // CG
KU = 3
NU = 1 + (KW - 2) // KU
HG = 5
NF = HC // HG
STORE_AFTER = (3, 6, 9, 12)
LOADS = 4
STORES = 2 * len(STORE_AFTER)
WEIGHT_DMAS = 5
LAG1, LAG2 = 2, 3

COLS = {}
_at = 0
for _name, _n in (("fwd_w", W), ("fwd_h", 2 * HC), ("inv_h", H), ("inv_w_even", W), ("inv_w_odd", W),
                  ("merge_even", H), ("merge_odd", H)):
    COLS[_name] = (_at, _at + _n)
    _at += _n
TABLE = _at


def transform_table():
    import numpy as np

    def cos(a, b):
        k = np.outer(a, b) % 128
        v = np.cos(2 * np.pi * k / 128)
        v[(k == 32) | (k == 96)] = 0.0
        return v

    def sin(a, b):
        return cos(a, b) * 0 + np.where(np.outer(a, b) % 64 == 0, 0.0, np.sin(2 * np.pi * (np.outer(a, b) % 128) / 128))

    n = np.arange(128)
    kw = np.arange(1, 64)
    kh = np.concatenate([np.arange(0, 65), -np.arange(1, 64)])
    fwd_w = np.zeros((128, 128))
    fwd_w[:, 0] = 1.0
    fwd_w[:, 1] = 1.0 - 2.0 * (n % 2)
    fwd_w[:, 2::2] = cos(n, kw)
    fwd_w[:, 3::2] = -sin(n, kw)
    half = np.arange(0, 65)
    fwd_h = np.concatenate([cos(n, half), sin(n, half)], 1)
    inv_h = np.concatenate([cos(kh, half), sin(kh, kw)], 1)
    inv_even = np.zeros((128, 128))
    inv_even[0] = 1.0
    inv_even[1] = 1.0 - 2.0 * (n % 2)
    inv_even[2::2] = 2.0 * cos(kw, n)
    inv_even[3::2] = -2.0 * sin(kw, n)
    inv_odd = np.zeros((128, 128))
    inv_odd[0] = -1.0
    inv_odd[1] = -(1.0 - 2.0 * (n % 2))
    inv_odd[2::2] = -2.0 * sin(kw, n)
    inv_odd[3::2] = -2.0 * cos(kw, n)
    flip = (kh[:, None] == -kh[None, :]) | ((kh[:, None] + kh[None, :]) == 128)
    eye = np.eye(128)
    merge_even = (eye + flip) / 2
    merge_odd = (eye - flip) / 2
    return np.concatenate([fwd_w / 128, fwd_h, inv_h, inv_even / 128, inv_odd / 128,
                           merge_even, merge_odd], 1).astype(np.float32)


def build(nc, x, w1, b1, w2, b2, table, out):
    with ExitStack() as ctx:
        def sb(name, shape, dt=F32):
            return ctx.enter_context(nc.sbuf_tensor(name, shape, dt))

        def sem(name):
            return ctx.enter_context(nc.semaphore(name))

        tab = sb("tab", [128, TABLE])
        xs = [sb(f"x{p}", [W, H, CB]) for p in range(PAIRS)]
        ydg = sb("ydg", [128, 128, CB])
        w1s = sb("w1s", [CB, 2, CB])
        w1hi = sb("w1hi", [CB, 3, CB], F32R)
        w1lo = sb("w1lo", [CB, 3, CB], F32R)
        b1s = sb("b1s", [CB, 2])
        w2r = sb("w2r", [CB + 1, 2, CB])
        w2i = sb("w2i", [CB, 2, CB])
        pcopy = [sb(f"pcopy{j}", [CB, KU, 2 * HC]) for j in range(2)]
        z = [sb(f"z{j}", [CB, 2, KU, H]) for j in range(2)]
        zhi = [sb(f"zhi{j}", [CB, 2, KU, H], F32R) for j in range(2)]
        zlo = [sb(f"zlo{j}", [CB, 2, KU, H], F32R) for j in range(2)]
        hid = [sb(f"hid{j}", [CB + 1, 2, KU, H]) for j in range(2)]
        clamped = [sb(f"clamped{j}", [128, KU, 2 * CB]) for j in range(2)]
        edge = sb("edge", [128, 2, 2, CB])
        vcopy = [sb(f"vcopy{j}", [W, HG, CB]) for j in range(3)]
        ps = ctx.enter_context(nc.psum_tensor("ps", [128, 8, 512], F32))

        table_loaded = sem("table_loaded")
        ones_set = sem("ones_set")
        x_loaded = [sem(f"x_loaded{p}") for p in range(PAIRS)]
        stored = [sem(f"stored{p}") for p in range(PAIRS)]
        weights_loaded = sem("weights_loaded")
        w1hi_ready = sem("w1hi_ready")
        w1lo_ready = sem("w1lo_ready")
        line_done = sem("line_done")
        line_act = sem("line_act")
        line_dve = sem("line_dve")
        p_done = sem("p_done")
        q_done = sem("q_done")
        p_copied = sem("p_copied")
        z_ready = sem("z_ready")
        zhi_ready = sem("zhi_ready")
        zlo_ready = sem("zlo_ready")
        mix1r_done = sem("mix1r_done")
        mix1i_done = sem("mix1i_done")
        hid_ready = sem("hid_ready")
        mix2_done = sem("mix2_done")
        clamp_done = sem("clamp_done")
        shrunk = sem("shrunk")
        merge_done = sem("merge_done")
        merged = sem("merged")
        u_done = sem("u_done")
        v_done = sem("v_done")
        v_copied = sem("v_copied")
        plus_ready = sem("plus_ready")
        minus_ready = sem("minus_ready")
        y_ready = sem("y_ready")

        def mat(name):
            a, b = COLS[name]
            return tab[:, a:b]

        O_BANK, M_BANK, E_BANK = 4, 6, 0
        M_STEP = 320
        mixed = ps[:, M_BANK:M_BANK + 2, :].rearrange("p b n -> p (b n)")[:, 0:3 * M_STEP].rearrange(
            "p (k n) -> p k n", k=KU)[:, :, 0:2 * CB]

        def p_bank(v):
            return 2 * (v % 2)

        def q_bank(v):
            return 2 * (v % 2) + 1

        def count(v):
            return KU if v else 2

        def kws(v):
            return 2 + KU * (v - 1) if v else 0

        def line_bank(stage, g):
            return (g + 2) % 8 if stage == 0 else g % 8

        def line_psum(bank):
            return ps[:, bank, :].rearrange("p (c k) -> p k c", c=CG)

        def odd_rows(g):
            return max(HG * g, 1), min(HG * g + HG, H // 2)

        def mirror(t, a, b):
            return t[:, H - a:H - b:-1, :]

        with nc.Block() as block:

            @block.sync
            def _(sp):
                sp.dma_start(tab[:], table).then_inc(table_loaded, 16)

                def load_x(n, b, p):
                    src = x[bass.ds(b, 1), :, :, bass.ds(n * CB, CB)].rearrange("o h w c -> (o w) h c")
                    for i in range(LOADS):
                        rows = slice(i * H // LOADS, (i + 1) * H // LOADS)
                        sp.dma_start(xs[p][:, rows, :], src[:, rows, :]).then_inc(x_loaded[p], 16)

                def load_weights(n):
                    one = bass.ds(n, 1)
                    sp.dma_start(w1s[:], w1[:, one].rearrange("r o i j -> (o i) r j")).then_inc(weights_loaded, 16)
                    sp.dma_start(b1s[:], b1[:, one].rearrange("r o (i z) -> (o i) r z", z=1)).then_inc(weights_loaded, 16)
                    sp.dma_start(w2r[0:CB], w2[:, one].rearrange("r o i j -> (o i) r j")).then_inc(weights_loaded, 16)
                    sp.dma_start(w2r[CB:CB + 1], b2[:, one].rearrange("r o j -> o r j")).then_inc(weights_loaded, 16)
                    sp.dma_start(w2i[:, 1, :], w2[0:1, one].rearrange("r o i j -> (r o i) j")).then_inc(weights_loaded, 16)

                with nc.allow_non_contiguous_dma(reason="biases, one element per partition"):
                    load_x(0, 0, 0)
                    load_weights(0)
                    load_x(0, 1, 1)
                    def step(t, last):
                        for p in range(PAIRS):
                            q = t * PAIRS + p
                            if p == PAIRS - 1 and not last:
                                sp.wait_ge(mix2_done, KW * q + KW)
                                load_weights((q + 1) // B)
                            b = q % B
                            dst = out[bass.ds(b, 1), :, :, bass.ds(q // B * CB, CB)].rearrange("o h w c -> (o w) h c")
                            a = 0
                            for g in STORE_AFTER:
                                e = HG * (g + 1)
                                sp.wait_ge(y_ready, NF * q + NF + g + 1)
                                sp.dma_start(dst[:, a:e, :], xs[p][:, a:e, :]).then_inc(stored[p], 16)
                                lo, hi = H - min(e, H // 2) + 1, H - max(a, 1) + 1
                                sp.dma_start(dst[:, lo:hi, :], xs[p][:, lo:hi, :]).then_inc(stored[p], 16)
                                a = e
                            sp.wait_ge(stored[p], (t + 1) * 16 * STORES)
                            if not last:
                                load_x((q + PAIRS) // B, (q + PAIRS) % B, p)

                    with sp.Fori(0, STEPS - 1) as t:
                        step(t, False)
                    step(STEPS - 1, True)

            @block.tensor
            def _(pe):
                def lines(q, t, p, stage):
                    src = xs[p] if stage == 0 else ydg
                    rhs = mat("fwd_w") if stage == 0 else mat("inv_h")
                    for g in range(NG):
                        bank = line_bank(stage, g)
                        if g >= 8:
                            freed = line_dve if g % 2 else line_act
                            pe.wait_ge(freed, NG * q + stage * NG // 2 + (g - 8) // 2 + 1)
                        elif stage == 0 and g % 2 == 0:
                            pe.wait_ge(y_ready, NF * q + NF - 4 + g // 2 + 1)
                        for j in range(CG):
                            mm = pe.matmul(ps[:, bank, j * 128:(j + 1) * 128], src[:, :, g * CG + j], rhs,
                                           start=True, stop=True)
                        mm.then_inc(line_done, 1)

                def lines_moved(q, stage):
                    n = NG * q + (stage + 1) * NG // 2
                    pe.wait_ge(line_act, n)
                    pe.wait_ge(line_dve, n)

                def fwd_h(q, v):
                    if v >= 2:
                        pe.wait_ge(z_ready, NU * q + v - 1)
                    for part in range(2 if v else 1):
                        bank = (p_bank, q_bank)[part](v)
                        for k in range(count(v)):
                            idx = 2 * (kws(v) + k - 1) + part if v else k
                            mm = pe.matmul(ps[0:CB, bank, k * 2 * HC:(k + 1) * 2 * HC], ydg[:, idx, :], mat("fwd_h"),
                                           start=True, stop=True)
                        mm.then_inc((p_done, q_done)[part], 1)

                def mix1(q, v):
                    pe.wait_ge(zlo_ready, NU * q + v + 1)
                    if v:
                        pe.wait_ge(hid_ready, NU * q + v)
                    n = count(v)
                    for i, (terms, done) in enumerate(((((0, 0), (2, 1)), mix1r_done), (((0, 1), (1, 0)), mix1i_done))):
                        passes = []
                        for wj, zj in terms:
                            hi, lo = zhi[v % 2][:, zj, 0:n, :], zlo[v % 2][:, zj, 0:n, :]
                            passes += [(w1lo[:, wj, :], hi), (w1hi[:, wj, :], lo), (w1hi[:, wj, :], hi)]
                        for j, (w, m) in enumerate(passes):
                            mm = pe.matmul(ps[0:CB, O_BANK + i, 0:n * H], w, m, start=(j == 0),
                                           stop=(j == len(passes) - 1))
                        mm.then_inc(done, 1)

                def mix2(q, v):
                    pe.wait_ge(hid_ready, NU * q + v + 1)
                    if v:
                        pe.wait_ge(shrunk, NU * q + v)
                    for k in range(count(v)):
                        o = mixed[:, k, :]
                        pe.matmul(o, hid[v % 2][:, 0, k, :], w2r[:].rearrange("p r c -> p (r c)"),
                                  start=True, stop=False)
                        pe.matmul(o, hid[v % 2][0:CB, 1, k, :], w2i[:].rearrange("p r c -> p (r c)"),
                                  start=False, stop=True).then_inc(mix2_done, 1)

                def merge(q):
                    pe.wait_ge(shrunk, NU * q + 1)
                    o = ps[:, E_BANK, 0:2 * CB].rearrange("p (k c) -> p k c", k=2)
                    pe.matmul(o, mat("merge_even"), edge[:, :, 0, :], start=True, stop=False)
                    pe.matmul(o, mat("merge_odd"), edge[:, :, 1, :], start=False, stop=True).then_inc(merge_done, 1)

                def rows(q, g):
                    bank = 2 * (g % 4)
                    if g >= 4:
                        pe.wait_ge(y_ready, NF * q + NF + g - 3)
                    a, b = odd_rows(g)
                    pe.matmul(ps[:, bank + 1, 0:(b - a) * CB], mat("inv_w_odd"),
                              ydg[:, HC + a - 1:HC + b - 1, :].rearrange("p h c -> p (h c)"),
                              start=True, stop=True).then_inc(v_done, 1)
                    pe.matmul(ps[:, bank, 0:HG * CB], mat("inv_w_even"),
                              ydg[:, HG * g:HG * g + HG, :].rearrange("p h c -> p (h c)"),
                              start=True, stop=True).then_inc(u_done, 1)

                pe.wait_ge(table_loaded, 16)
                pe.wait_ge(ones_set, 2)
                with pe.Fori(0, STEPS) as t:
                    for p in range(PAIRS):
                        q = t * PAIRS + p
                        pe.wait_ge(x_loaded[p], (t + 1) * 16 * LOADS)
                        lines(q, t, p, 0)
                        lines_moved(q, 0)
                        if p == 0:
                            pe.wait_ge(w1hi_ready, t + 1)
                            pe.wait_ge(w1lo_ready, t + 1)
                        for v in range(NU + LAG2):
                            if v < NU:
                                fwd_h(q, v)
                            if LAG1 <= v < NU + LAG1:
                                mix1(q, v - LAG1)
                            if v >= LAG2:
                                mix2(q, v - LAG2)
                        merge(q)
                        pe.wait_ge(shrunk, NU * q + NU)
                        pe.wait_ge(merged, q + 1)
                        lines(q, t, p, 1)
                        lines_moved(q, 1)
                        for g in range(NF):
                            rows(q, g)

            @block.scalar
            def _(act):
                def lines(q, stage):
                    for g in range(0, NG, 2):
                        act.wait_ge(line_done, 2 * NG * q + stage * NG + g + 1)
                        act.copy(ydg[:, :, g * CG:(g + 1) * CG], line_psum(line_bank(stage, g))).then_inc(line_act, 1)

                act.wait_ge(ones_set, 2)
                with act.Fori(0, STEPS) as t:
                    for p in range(PAIRS):
                        q = t * PAIRS + p
                        lines(q, 0)
                        if p == 0:
                            act.wait_ge(weights_loaded, (t + 1) * 16 * WEIGHT_DMAS)
                            act.copy(w1hi[:, 0:2, :], w1s[:])
                            act.mul(w1hi[:, 2, :], w1s[:, 1, :], -1.0)
                            act.mul(w2i[:, 0, :], w2r[0:CB, 1, :], -1.0).then_inc(w1hi_ready, 1)
                        for v in range(NU + LAG1):
                            if 1 <= v < NU:
                                act.wait_ge(p_done, NU * q + v + 1)
                                if v >= 2:
                                    act.wait_ge(z_ready, NU * q + v - 1)
                                act.copy(pcopy[v % 2][:].rearrange("p k n -> p (k n)"),
                                         ps[0:CB, p_bank(v), 0:KU * 2 * HC]).then_inc(p_copied, 1)
                            if v < NU:
                                act.wait_ge(z_ready, NU * q + v + 1)
                                if v >= 2:
                                    act.wait_ge(mix1i_done, NU * q + v - 1)
                                act.copy(zhi[v % 2][:, :, 0:count(v), :], z[v % 2][:, :, 0:count(v), :]).then_inc(zhi_ready, 1)
                            if v >= LAG1:
                                u = v - LAG1
                                n = count(u) * H
                                if u >= 2:
                                    act.wait_ge(mix2_done, KW * q + kws(u - 1))
                                for i in range(2):
                                    act.wait_ge((mix1r_done, mix1i_done)[i], NU * q + u + 1)
                                    ins = act.activation(hid[u % 2][0:CB, i].rearrange("p k n -> p (k n)")[:, 0:n],
                                                         ps[0:CB, O_BANK + i, 0:n], ACT.Relu, bias=b1s[:, i:i + 1])
                                ins.then_inc(hid_ready, 1)
                        act.wait_ge(merge_done, q + 1)
                        act.copy(ydg[:, 0:2, :].rearrange("p k c -> p (k c)"),
                                 ps[:, E_BANK, 0:2 * CB]).then_inc(merged, 1)
                        lines(q, 1)
                        for g in range(NF):
                            act.wait_ge(v_done, NF * q + g + 1)
                            if g >= 3:
                                act.wait_ge(y_ready, NF * q + NF + g - 2)
                            a, b = odd_rows(g)
                            act.copy(vcopy[g % 3][:, 0:b - a, :].rearrange("p h c -> p (h c)"),
                                     ps[:, 2 * (g % 4) + 1, 0:(b - a) * CB]).then_inc(v_copied, 1)

            @block.vector
            def _(dve):
                def lines(q, stage):
                    for g in range(1, NG, 2):
                        dve.wait_ge(line_done, 2 * NG * q + stage * NG + g + 1)
                        dve.tensor_copy(ydg[:, :, g * CG:(g + 1) * CG],
                                        line_psum(line_bank(stage, g))).then_inc(line_dve, 1)

                def modes(q, v):
                    zr, zi = z[v % 2][:, 0], z[v % 2][:, 1]
                    if v >= 2:
                        dve.wait_ge(zlo_ready, NU * q + v - 1)
                    if v == 0:
                        dve.wait_ge(p_done, NU * q + 1)
                        pp = ps[0:CB, p_bank(0), 0:2 * 2 * HC].rearrange("p (k n) -> p k n", k=2)
                        dve.tensor_copy(zr[:, 0:2, 0:HC], pp[:, :, 0:HC])
                        dve.tensor_copy(zr[:, 0:2, HC:H], pp[:, :, 1:HC - 1])
                        dve.tensor_scalar(zi[:, 0:2, 0:HC], pp[:, :, HC:2 * HC], -1.0, None, ALU.mult)
                        dve.tensor_copy(zi[:, 0:2, HC:H], pp[:, :, HC + 1:2 * HC - 1]).then_inc(z_ready, 1)
                        return
                    pc = pcopy[v % 2]
                    pq = ps[0:CB, q_bank(v), 0:KU * 2 * HC].rearrange("p (k n) -> p k n", k=KU)
                    dve.wait_ge(p_copied, (NU - 1) * q + v)
                    dve.wait_ge(q_done, (NU - 1) * q + v)
                    dve.tensor_tensor(zr[:, :, 0:HC], pq[:, :, HC:2 * HC], pc[:, :, 0:HC], ALU.add)
                    dve.tensor_tensor(zr[:, :, HC:H], pc[:, :, 1:HC - 1], pq[:, :, HC + 1:2 * HC - 1], ALU.subtract)
                    dve.tensor_tensor(zi[:, :, 0:HC], pq[:, :, 0:HC], pc[:, :, HC:2 * HC], ALU.subtract)
                    dve.tensor_tensor(zi[:, :, HC:H], pq[:, :, 1:HC - 1], pc[:, :, HC + 1:2 * HC - 1],
                                      ALU.add).then_inc(z_ready, 1)

                def shrink(q, v):
                    if v >= 2:
                        dve.wait_ge(shrunk, NU * q + v - 1)
                    pieces = [(0, 2), (2, 3)] if v == NU - 1 else [(0, count(v))]
                    for j, (a, b) in enumerate(pieces):
                        d, c = mixed[:, a:b, :], clamped[v % 2][:, a:b, :]
                        if v:
                            lo = 2 * (kws(v) - 1)
                            dst = ydg[:, lo + 2 * a:lo + 2 * b, :].rearrange("p (k r) c -> p k (r c)", r=2)
                        else:
                            dst = edge[:].rearrange("p k r c -> p k (r c)")
                        dve.wait_ge(mix2_done, KW * q + kws(v) + b)
                        dve.tensor_scalar(c, d, LAMBD, -LAMBD, ALU.min, ALU.max).then_inc(clamp_done, 1)
                        dve.wait_ge(clamp_done, (NU + 1) * q + v + j + 1)
                        ins = dve.tensor_tensor(dst, d, c, ALU.subtract)
                    ins.then_inc(shrunk, 1)

                def finish(q, p, g):
                    a, b = odd_rows(g)
                    xm = mirror(xs[p], a, b)
                    u = ps[:, 2 * (g % 4), 0:HG * CB].rearrange("p (h c) -> p h c", c=CB)
                    dve.wait_ge(v_copied, NF * q + g + 1)
                    dve.tensor_tensor(xm, xm, vcopy[g % 3][:, 0:b - a, :], ALU.subtract).then_inc(minus_ready, 1)
                    xp = xs[p][:, HG * g:HG * g + HG, :]
                    dve.wait_ge(u_done, NF * q + g + 1)
                    dve.wait_ge(plus_ready, NF * q + g + 1)
                    dve.tensor_tensor(xp, u, xp, ALU.add)
                    dve.wait_ge(minus_ready, NF * q + g + 1)
                    dve.tensor_tensor(xm, u[:, a - HG * g:b - HG * g, :], xm, ALU.add).then_inc(y_ready, 1)

                dve.memset(hid[0][CB:CB + 1, 0], 1.0).then_inc(ones_set, 1)
                dve.memset(hid[1][CB:CB + 1, 0], 1.0).then_inc(ones_set, 1)
                dve.memset(clamped[0][0:1, 0, 0:1], 0.0).then_inc(y_ready, NF)
                dve.wait_ge(y_ready, NF)
                with dve.Fori(0, STEPS) as t:
                    for p in range(PAIRS):
                        q = t * PAIRS + p
                        lines(q, 0)
                        for v in range(NU + LAG2):
                            if v < NU:
                                modes(q, v)
                            if v >= LAG2:
                                shrink(q, v - LAG2)
                        lines(q, 1)
                        for g in range(NF):
                            finish(q, p, g)

            @block.gpsimd
            def _(pool):
                with pool.Fori(0, STEPS) as t:
                    pool.wait_ge(w1hi_ready, t + 1)
                    pool.tensor_tensor(w1lo[:, 0:2, :], w1s[:], w1hi[:, 0:2, :], ALU.subtract)
                    pool.tensor_tensor(w1lo[:, 2, :], w1hi[:, 1, :], w1s[:, 1, :], ALU.subtract).then_inc(w1lo_ready, 1)
                    for p in range(PAIRS):
                        q = t * PAIRS + p
                        for v in range(NU):
                            pool.wait_ge(zhi_ready, NU * q + v + 1)
                            if v >= 2:
                                pool.wait_ge(mix1i_done, NU * q + v - 1)
                            n = count(v)
                            pool.tensor_tensor(zlo[v % 2][:, :, 0:n, :], z[v % 2][:, :, 0:n, :],
                                               zhi[v % 2][:, :, 0:n, :], ALU.subtract).then_inc(zlo_ready, 1)
                        for g in range(NF):
                            a, b = odd_rows(g)
                            xp = xs[p][:, a:b, :]
                            pool.wait_ge(v_copied, NF * q + g + 1)
                            pool.tensor_tensor(xp, xp, vcopy[g % 3][:, 0:b - a, :], ALU.add).then_inc(plus_ready, 1)


def kernel(x, L0_conv_w1, L0_conv_b1, L0_conv_w2, L0_conv_b2):
    import numpy as np
    import concourse.bacc as bacc
    from concourse.bass_utils import run_bass_kernel_spmd

    nc = bacc.Bacc("TRN2", target_bir_lowering=False, num_devices=1)
    arrays = {"x": x, "w1": L0_conv_w1, "b1": L0_conv_b1, "w2": L0_conv_w2, "b2": L0_conv_b2,
              "table": transform_table()}
    arrays = {name: np.ascontiguousarray(a) for name, a in arrays.items()}
    args = [nc.dram_tensor(f"in_{name}", a.shape, mybir.dt.from_np(a.dtype), kind="ExternalInput").ap()
            for name, a in arrays.items()]
    out = nc.dram_tensor("out", (B, H, W, C), F32, kind="ExternalOutput").ap()
    build(nc, *args, out)
    r = run_bass_kernel_spmd(nc, [{f"in_{name}": a for name, a in arrays.items()}], core_ids=[0])
    return r.results[0]["out"]
```

```python
from contextlib import ExitStack

import concourse.bass as bass
from concourse import mybir

ACT = mybir.ActivationFunctionType
ALU = mybir.AluOpType
F32 = mybir.dt.float32
F32R = mybir.dt.float32r

B, H, W, C = 4, 128, 128, 768
NB = 8
CB = C // NB
LAMBD = 0.01
HC = H // 2 + 1
HS = H // 2 - 1
KW = W // 2 + 1
PAIRS = 2
STEPS = B * NB // PAIRS

CG = 4
LINE_SIZES = [CG] * 22 + [3, 2, 2, 1]
LINE_GROUPS = [(sum(LINE_SIZES[:i]), n) for i, n in enumerate(LINE_SIZES)]
NG = len(LINE_GROUPS)
assert sum(LINE_SIZES) == CB and NG % 2 == 0
KU = 3
NU = 1 + (KW - 2) // KU
HG = 5
NF = HC // HG
STORE_AFTER = (1, 3, 5, 7, 9, 11, 12)
LOADS = 4
STORES = 2 * len(STORE_AFTER)
WEIGHT_DMAS = 6
LAG1, LAG2 = 2, 3
WHOLE = (0, 1)
SPLIT = [v for v in range(NU) if v not in WHOLE]
DVE_SPLITS = (2,)
POOL_SPLITS = [v for v in SPLIT if v not in DVE_SPLITS]
SUM_LAST = 0
LOW_BANKS = (NU - 3, NU - 1)

COLS = {}
_at = 0
for _name, _n in (("fwd_w", W), ("fwd_h", 2 * HC), ("inv_h", H), ("inv_w_even", W), ("inv_w_odd", W),
                  ("merge_even", H), ("merge_odd", H)):
    COLS[_name] = (_at, _at + _n)
    _at += _n
TABLE = _at


def transform_table():
    import numpy as np

    def cos(a, b):
        k = np.outer(a, b) % 128
        v = np.cos(2 * np.pi * k / 128)
        v[(k == 32) | (k == 96)] = 0.0
        return v

    def sin(a, b):
        return cos(a, b) * 0 + np.where(np.outer(a, b) % 64 == 0, 0.0, np.sin(2 * np.pi * (np.outer(a, b) % 128) / 128))

    n = np.arange(128)
    kw = np.arange(1, 64)
    kh = np.concatenate([np.arange(0, 65), -np.arange(1, 64)])
    fwd_w = np.zeros((128, 128))
    fwd_w[:, 0] = 1.0
    fwd_w[:, 1] = 1.0 - 2.0 * (n % 2)
    fwd_w[:, 2::2] = cos(n, kw)
    fwd_w[:, 3::2] = -sin(n, kw)
    half = np.arange(0, 65)
    fwd_h = np.concatenate([cos(n, half), sin(n, half)], 1)
    inv_h = np.concatenate([cos(kh, half), sin(kh, kw)], 1)
    inv_even = np.zeros((128, 128))
    inv_even[0] = 1.0
    inv_even[1] = 1.0 - 2.0 * (n % 2)
    inv_even[2::2] = 2.0 * cos(kw, n)
    inv_even[3::2] = -2.0 * sin(kw, n)
    inv_odd = np.zeros((128, 128))
    inv_odd[0] = -1.0
    inv_odd[1] = -(1.0 - 2.0 * (n % 2))
    inv_odd[2::2] = -2.0 * sin(kw, n)
    inv_odd[3::2] = -2.0 * cos(kw, n)
    flip = (kh[:, None] == -kh[None, :]) | ((kh[:, None] + kh[None, :]) == 128)
    eye = np.eye(128)
    merge_even = (eye + flip) / 2
    merge_odd = (eye - flip) / 2
    return np.concatenate([fwd_w / 128, fwd_h, inv_h, inv_even / 128, inv_odd / 128,
                           merge_even, merge_odd], 1).astype(np.float32)


def build(nc, x, w1, b1, w2, b2, table, out):
    with ExitStack() as ctx:
        def sb(name, shape, dt=F32):
            return ctx.enter_context(nc.sbuf_tensor(name, shape, dt))

        def sem(name):
            return ctx.enter_context(nc.semaphore(name))

        tab = sb("tab", [128, TABLE])
        xs = [sb(f"x{p}", [W, H, CB]) for p in range(PAIRS)]
        ydg = sb("ydg", [128, 128, CB])
        w1i = sb("w1i", [CB, CB])
        w1g = sb("w1g", [CB, 3, CB])
        w1hi = sb("w1hi", [CB, 3, CB], F32R)
        w1lo = sb("w1lo", [CB, 3, CB], F32R)
        b1s = sb("b1s", [CB, 2])
        w2r = sb("w2r", [CB + 1, 2, CB])
        w2i = sb("w2i", [CB, 2, CB])
        pcopy = [sb(f"pcopy{j}", [CB, KU, 2 * HC]) for j in range(2)]
        z = [sb(f"z{j}", [CB, 3, KU, H]) for j in range(2)]
        zhi = [sb(f"zhi{j}", [CB, 3, KU, H], F32R) for j in range(2)]
        zlo = [sb(f"zlo{j}", [CB, 3, KU, H], F32R) for j in range(2)]
        tcopy = [sb(f"tcopy{j}", [CB, KU * H]) for j in range(2)]
        hid = [sb(f"hid{j}", [CB + 1, 2, KU * H]) for j in range(2)]
        clamped = [sb(f"clamped{j}", [128, KU, 2 * CB]) for j in range(2)]
        edge = sb("edge", [128, 2, 2, CB])
        vcopy = [sb(f"vcopy{j}", [W, HG, CB]) for j in range(3)]
        ps = ctx.enter_context(nc.psum_tensor("ps", [128, 8, 512], F32))

        fwd_w_loaded = sem("fwd_w_loaded")
        table_loaded = sem("table_loaded")
        ones_set = sem("ones_set")
        x_loaded = [sem(f"x_loaded{p}") for p in range(PAIRS)]
        stored = [sem(f"stored{p}") for p in range(PAIRS)]
        weights_loaded = sem("weights_loaded")
        w1g_ready = sem("w1g_ready")
        w1hi_ready = sem("w1hi_ready")
        w1lo_ready = sem("w1lo_ready")
        line_done = sem("line_done")
        line_act = sem("line_act")
        line_dve = sem("line_dve")
        p_done = sem("p_done")
        q_done = sem("q_done")
        p_copied = sem("p_copied")
        z_ready = sem("z_ready")
        zsum_ready = sem("zsum_ready")
        zhi_ready = sem("zhi_ready")
        zsum_hi_ready = sem("zsum_hi_ready")
        zlo_ready = sem("zlo_ready")
        zlo_dve_ready = sem("zlo_dve_ready")
        zsum_lo_ready = sem("zsum_lo_ready")
        t_done = sem("t_done")
        r_done = sem("r_done")
        mix1_done = sem("mix1_done")
        t_copied = sem("t_copied")
        mixed_ready = sem("mixed_ready")
        hid_ready = sem("hid_ready")
        mix2_done = sem("mix2_done")
        clamp_done = sem("clamp_done")
        shrunk = sem("shrunk")
        merge_done = sem("merge_done")
        merged = sem("merged")
        u_done = sem("u_done")
        v_done = sem("v_done")
        v_copied = sem("v_copied")
        plus_ready = sem("plus_ready")
        minus_ready = sem("minus_ready")
        y_ready = sem("y_ready")

        def mat(name):
            a, b = COLS[name]
            return tab[:, a:b]

        T_BANK, R_BANK, I_BANK, M_BANK = 2, 3, 4, 5
        E_BANK = T_BANK
        M_STEP = 320

        def p_bank(v):
            return {0: M_BANK, 2: M_BANK + 1}.get(v, 0)

        def q_bank(v):
            return 7 if v % 2 else 1

        def mixed2(v, a, b):
            bank = 0 if v in LOW_BANKS else M_BANK
            return ps[:, bank:bank + 2, :].rearrange("p b n -> p (b n)")[:, 0:KU * M_STEP].rearrange(
                "p (k n) -> p k n", k=KU)[:, a:b, 0:2 * CB]

        def split_count(q, v):
            return len(SPLIT) * q + SPLIT.index(v) + 1

        def wait_zlo(engine, q, v):
            if v in DVE_SPLITS:
                engine.wait_ge(zlo_dve_ready, len(DVE_SPLITS) * q + DVE_SPLITS.index(v) + 1)
            else:
                engine.wait_ge(zlo_ready, len(POOL_SPLITS) * q + POOL_SPLITS.index(v) + 1)

        def count(v):
            return KU if v else 2

        def kws(v):
            return 2 + KU * (v - 1) if v else 0

        def line_bank(stage, g):
            return (g + 2) % 8 if stage == 0 else g % 8

        def line_moves(stage, g):
            c, n = LINE_GROUPS[g]
            return ydg[:, :, c:c + n], ps[:, line_bank(stage, g), 0:n * 128].rearrange("p (c k) -> p k c", c=n)

        def odd_rows(g):
            return max(HG * g, 1), min(HG * g + HG, H // 2)

        def mirror(t, a, b):
            return t[:, H - a:H - b:-1, :]

        with nc.Block() as block:

            @block.sync
            def _(sp):
                sp.dma_start(tab[:, 0:W], table[:, 0:W]).then_inc(fwd_w_loaded, 16)

                def load_x(n, b, p):
                    src = x[bass.ds(b, 1), :, :, bass.ds(n * CB, CB)].rearrange("o h w c -> (o w) h c")
                    for i in range(LOADS):
                        rows = slice(i * H // LOADS, (i + 1) * H // LOADS)
                        sp.dma_start(xs[p][:, rows, :], src[:, rows, :]).then_inc(x_loaded[p], 16)

                def load_weights(n):
                    one = bass.ds(n, 1)
                    sp.dma_start(w1g[:, 0, :], w1[0:1, one].rearrange("r o i j -> (r o i) j")).then_inc(weights_loaded, 16)
                    sp.dma_start(w1i[:], w1[1:2, one].rearrange("r o i j -> (r o i) j")).then_inc(weights_loaded, 16)
                    sp.dma_start(b1s[:], b1[:, one].rearrange("r o (i z) -> (o i) r z", z=1)).then_inc(weights_loaded, 16)
                    sp.dma_start(w2r[0:CB], w2[:, one].rearrange("r o i j -> (o i) r j")).then_inc(weights_loaded, 16)
                    sp.dma_start(w2r[CB:CB + 1], b2[:, one].rearrange("r o j -> o r j")).then_inc(weights_loaded, 16)
                    sp.dma_start(w2i[:, 1, :], w2[0:1, one].rearrange("r o i j -> (r o i) j")).then_inc(weights_loaded, 16)

                with nc.allow_non_contiguous_dma(reason="biases, one element per partition"):
                    load_x(0, 0, 0)
                    sp.dma_start(tab[:, W:TABLE], table[:, W:TABLE]).then_inc(table_loaded, 16)
                    load_weights(0)
                    load_x(0, 1, 1)

                    def step(t, last):
                        for p in range(PAIRS):
                            q = t * PAIRS + p
                            if p == PAIRS - 1 and not last:
                                sp.wait_ge(mix2_done, KW * q + KW)
                                load_weights((q + 1) // B)
                            b = q % B
                            dst = out[bass.ds(b, 1), :, :, bass.ds(q // B * CB, CB)].rearrange("o h w c -> (o w) h c")
                            a = 0
                            for g in STORE_AFTER:
                                e = HG * (g + 1)
                                sp.wait_ge(y_ready, NF * q + NF + g + 1)
                                sp.dma_start(dst[:, a:e, :], xs[p][:, a:e, :]).then_inc(stored[p], 16)
                                lo, hi = H - min(e, H // 2) + 1, H - max(a, 1) + 1
                                sp.dma_start(dst[:, lo:hi, :], xs[p][:, lo:hi, :]).then_inc(stored[p], 16)
                                a = e
                            sp.wait_ge(stored[p], (t + 1) * 16 * STORES)
                            if not last:
                                load_x((q + PAIRS) // B, (q + PAIRS) % B, p)

                    with sp.Fori(0, STEPS - 1) as t:
                        step(t, False)
                    step(STEPS - 1, True)

            @block.tensor
            def _(pe):
                def lines(q, p, stage):
                    src = xs[p] if stage == 0 else ydg
                    rhs = mat("fwd_w") if stage == 0 else mat("inv_h")
                    for g in range(NG):
                        bank = line_bank(stage, g)
                        if g >= 8:
                            freed = line_dve if g % 2 else line_act
                            pe.wait_ge(freed, NG * q + stage * (NG // 2) + (g - 8) // 2 + 1)
                        elif stage == 0 and g % 2 == 0:
                            pe.wait_ge(y_ready, NF * q + NF - 4 + g // 2 + 1)
                        c, size = LINE_GROUPS[g]
                        for j in range(size):
                            mm = pe.matmul(ps[:, bank, j * 128:(j + 1) * 128], src[:, :, c + j], rhs,
                                           start=True, stop=True)
                        mm.then_inc(line_done, 1)

                def lines_moved(q, stage):
                    n = NG * q + (stage + 1) * (NG // 2)
                    pe.wait_ge(line_act, n)
                    pe.wait_ge(line_dve, n)

                def fwd_h(q, v):
                    for part in range(2 if v else 1):
                        if part == 0 and v >= 3:
                            pe.wait_ge(p_copied, (NU - 1) * q + v - 1)
                        if part == 1 and v >= 3:
                            pe.wait_ge(z_ready, NU * q + v - 1)
                        bank = (p_bank, q_bank)[part](v)
                        for k in range(count(v)):
                            idx = 2 * (kws(v) + k - 1) + part if v else k
                            mm = pe.matmul(ps[0:CB, bank, k * 2 * HC:(k + 1) * 2 * HC], ydg[:, idx, :], mat("fwd_h"),
                                           start=True, stop=True)
                        mm.then_inc((p_done, q_done)[part], 1)

                def mix1(q, v):
                    if v:
                        pe.wait_ge(mixed_ready, 2 * (NU * q + v))

                    def product(j, bank):
                        o = ps[0:CB, bank, 0:count(v) * H]
                        if v in WHOLE:
                            return pe.matmul(o, w1g[:, j, :], z[v % 2][:, j, 0:count(v), :], start=True, stop=True)
                        hi, lo = zhi[v % 2][:, j, 0:count(v), :], zlo[v % 2][:, j, 0:count(v), :]
                        pe.matmul(o, w1lo[:, j, :], hi, start=True, stop=False)
                        pe.matmul(o, w1hi[:, j, :], lo, start=False, stop=False)
                        return pe.matmul(o, w1hi[:, j, :], hi, start=False, stop=True)

                    def wait_sum():
                        if v in WHOLE:
                            pe.wait_ge(zsum_ready, NU * q + v + 1)
                        else:
                            pe.wait_ge(zsum_lo_ready, split_count(q, v))

                    if v != SUM_LAST:
                        wait_sum()
                        product(0, T_BANK).then_inc(t_done, 1)
                    if v in WHOLE:
                        pe.wait_ge(z_ready, NU * q + v + 1)
                    else:
                        wait_zlo(pe, q, v)
                    product(1, R_BANK).then_inc(r_done, 1)
                    last = product(2, I_BANK)
                    if v == SUM_LAST:
                        wait_sum()
                        last = product(0, T_BANK)
                    last.then_inc(mix1_done, 1)

                def mix2(q, v):
                    pe.wait_ge(hid_ready, NU * q + v + 1)
                    if v == LOW_BANKS[0]:
                        pe.wait_ge(p_copied, (NU - 1) * (q + 1))
                    elif v:
                        pe.wait_ge(shrunk, NU * q + (v - 1 if v > LOW_BANKS[0] else v))
                    for k in range(count(v)):
                        o = mixed2(v, k, k + 1)[:, 0, :]
                        pe.matmul(o, hid[v % 2][:, 0, k * H:(k + 1) * H], w2r[:].rearrange("p r c -> p (r c)"),
                                  start=True, stop=False)
                        pe.matmul(o, hid[v % 2][0:CB, 1, k * H:(k + 1) * H], w2i[:].rearrange("p r c -> p (r c)"),
                                  start=False, stop=True).then_inc(mix2_done, 1)

                def merge(q):
                    pe.wait_ge(shrunk, NU * q + 1)
                    o = ps[:, E_BANK, 0:2 * CB].rearrange("p (k c) -> p k c", k=2)
                    pe.matmul(o, mat("merge_even"), edge[:, :, 0, :], start=True, stop=False)
                    pe.matmul(o, mat("merge_odd"), edge[:, :, 1, :], start=False, stop=True).then_inc(merge_done, 1)

                def rows(q, g):
                    bank = 2 * (g % 4)
                    if g >= 4:
                        pe.wait_ge(y_ready, NF * q + NF + g - 3)
                    a, b = odd_rows(g)
                    pe.matmul(ps[:, bank + 1, 0:(b - a) * CB], mat("inv_w_odd"),
                              ydg[:, HC + a - 1:HC + b - 1, :].rearrange("p h c -> p (h c)"),
                              start=True, stop=True).then_inc(v_done, 1)
                    pe.matmul(ps[:, bank, 0:HG * CB], mat("inv_w_even"),
                              ydg[:, HG * g:HG * g + HG, :].rearrange("p h c -> p (h c)"),
                              start=True, stop=True).then_inc(u_done, 1)

                pe.wait_ge(fwd_w_loaded, 16)
                pe.wait_ge(ones_set, 2)
                with pe.Fori(0, STEPS) as t:
                    for p in range(PAIRS):
                        q = t * PAIRS + p
                        pe.wait_ge(x_loaded[p], (t + 1) * 16 * LOADS)
                        lines(q, p, 0)
                        pe.wait_ge(table_loaded, 16)
                        lines_moved(q, 0)
                        for v in range(NU + LAG2):
                            if v < NU:
                                fwd_h(q, v)
                            if LAG1 < v < NU + LAG1:
                                mix1(q, v - LAG1)
                            if v == LAG1 - 1:
                                if p == 0:
                                    pe.wait_ge(w1hi_ready, t + 1)
                                    pe.wait_ge(w1lo_ready, t + 1)
                                mix1(q, 0)
                            if v >= LAG2:
                                mix2(q, v - LAG2)
                        merge(q)
                        pe.wait_ge(shrunk, NU * q + NU)
                        pe.wait_ge(merged, q + 1)
                        lines(q, p, 1)
                        lines_moved(q, 1)
                        for g in range(NF):
                            rows(q, g)

            @block.scalar
            def _(act):
                def lines(q, stage):
                    for g in range(0, NG, 2):
                        act.wait_ge(line_done, 2 * NG * q + stage * NG + g + 1)
                        act.copy(*line_moves(stage, g)).then_inc(line_act, 1)

                def copy_p(q, v):
                    act.wait_ge(p_done, NU * q + v + 1)
                    if v >= 3:
                        act.wait_ge(z_ready, NU * q + v - 1)
                    act.copy(pcopy[v % 2][:].rearrange("p k n -> p (k n)"),
                             ps[0:CB, p_bank(v), 0:KU * 2 * HC]).then_inc(p_copied, 1)

                def split_high(q, v):
                    act.wait_ge(z_ready, NU * q + v + 1)
                    if v - 2 in SPLIT:
                        act.wait_ge(mix1_done, NU * q + v - 1)
                    k = count(v)
                    act.copy(zhi[v % 2][:, 1:3, 0:k, :], z[v % 2][:, 1:3, 0:k, :]).then_inc(zhi_ready, 1)

                def split_sum_high(q, v):
                    act.wait_ge(zsum_ready, NU * q + v + 1)
                    k = count(v)
                    act.copy(zhi[v % 2][:, 0, 0:k, :], z[v % 2][:, 0, 0:k, :]).then_inc(zsum_hi_ready, 1)

                def copy_t(q, u):
                    if u == SUM_LAST:
                        act.wait_ge(mix1_done, NU * q + u + 1)
                    else:
                        act.wait_ge(t_done, (NU - 1) * q + u)
                    if u >= 2:
                        act.wait_ge(mixed_ready, 2 * (NU * q + u - 1))
                    n = count(u) * H
                    act.copy(tcopy[u % 2][:, 0:n], ps[0:CB, T_BANK, 0:n]).then_inc(t_copied, 1)

                def relu(q, u):
                    for i in range(2):
                        act.wait_ge(mixed_ready, 2 * (NU * q + u) + i + 1)
                        h = hid[u % 2][0:CB, i, 0:count(u) * H]
                        ins = act.activation(h, h, ACT.Relu, bias=b1s[:, i:i + 1])
                    ins.then_inc(hid_ready, 1)

                act.wait_ge(ones_set, 2)
                with act.Fori(0, STEPS) as t:
                    for p in range(PAIRS):
                        q = t * PAIRS + p
                        lines(q, 0)
                        if p == 0:
                            act.wait_ge(weights_loaded, (t + 1) * 16 * WEIGHT_DMAS)
                            act.mul(w2i[:, 0, :], w2r[0:CB, 1, :], -1.0)
                            act.wait_ge(w1g_ready, t + 1)
                            act.copy(w1hi[:], w1g[:]).then_inc(w1hi_ready, 1)
                        copy_p(q, 1)
                        copy_t(q, 0)
                        copy_p(q, 2)
                        relu(q, 0)
                        copy_p(q, 3)
                        split_high(q, 2)
                        split_sum_high(q, 2)
                        copy_t(q, 1)
                        split_high(q, 3)
                        split_sum_high(q, 3)
                        relu(q, 1)
                        for v in range(4, NU + LAG1):
                            if v < NU:
                                copy_p(q, v)
                            copy_t(q, v - LAG1)
                            if v < NU:
                                split_high(q, v)
                                split_sum_high(q, v)
                            relu(q, v - LAG1)
                        act.wait_ge(merge_done, q + 1)
                        act.copy(ydg[:, 0:2, :].rearrange("p k c -> p (k c)"),
                                 ps[:, E_BANK, 0:2 * CB]).then_inc(merged, 1)
                        lines(q, 1)
                        for g in range(NF):
                            act.wait_ge(v_done, NF * q + g + 1)
                            if g >= 3:
                                act.wait_ge(y_ready, NF * q + NF + g - 2)
                            a, b = odd_rows(g)
                            act.copy(vcopy[g % 3][:, 0:b - a, :].rearrange("p h c -> p (h c)"),
                                     ps[:, 2 * (g % 4) + 1, 0:(b - a) * CB]).then_inc(v_copied, 1)

            @block.vector
            def _(dve):
                def lines(q, stage):
                    for g in range(1, NG, 2):
                        dve.wait_ge(line_done, 2 * NG * q + stage * NG + g + 1)
                        dve.tensor_copy(*line_moves(stage, g)).then_inc(line_dve, 1)

                def modes(q, v):
                    zr, zi = z[v % 2][:, 2], z[v % 2][:, 1]
                    if v >= 2:
                        if v - 2 in WHOLE:
                            dve.wait_ge(mix1_done, NU * q + v - 1)
                        else:
                            wait_zlo(dve, q, v - 2)
                            dve.wait_ge(zsum_lo_ready, split_count(q, v - 2))
                    if v == 0:
                        dve.wait_ge(p_done, NU * q + 1)
                        pp = ps[0:CB, p_bank(0), 0:2 * 2 * HC].rearrange("p (k n) -> p k n", k=2)
                        dve.tensor_copy(zr[:, 0:2, 0:HC], pp[:, :, 0:HC])
                        dve.tensor_copy(zr[:, 0:2, HC:H], pp[:, :, 1:HC - 1])
                        dve.tensor_scalar(zi[:, 0:2, 0:HC], pp[:, :, HC:2 * HC], -1.0, None, ALU.mult)
                        dve.tensor_copy(zi[:, 0:2, HC:H], pp[:, :, HC + 1:2 * HC - 1]).then_inc(z_ready, 1)
                        return
                    pc = pcopy[v % 2]
                    pq = ps[0:CB, q_bank(v), 0:KU * 2 * HC].rearrange("p (k n) -> p k n", k=KU)
                    dve.wait_ge(p_copied, (NU - 1) * q + v)
                    dve.wait_ge(q_done, (NU - 1) * q + v)
                    dve.tensor_tensor(zr[:, :, 0:HC], pq[:, :, HC:2 * HC], pc[:, :, 0:HC], ALU.add)
                    dve.tensor_tensor(zr[:, :, HC:H], pc[:, :, 1:HC - 1], pq[:, :, HC + 1:2 * HC - 1], ALU.subtract)
                    dve.tensor_tensor(zi[:, :, 0:HC], pq[:, :, 0:HC], pc[:, :, HC:2 * HC], ALU.subtract)
                    dve.tensor_tensor(zi[:, :, HC:H], pq[:, :, 1:HC - 1], pc[:, :, HC + 1:2 * HC - 1],
                                      ALU.add).then_inc(z_ready, 1)

                def split_low(q, v):
                    dve.wait_ge(zhi_ready, split_count(q, v))
                    dve.wait_ge(z_ready, NU * q + v + 1)
                    k = count(v)
                    dve.tensor_tensor(zlo[v % 2][:, 1:3, 0:k, :], z[v % 2][:, 1:3, 0:k, :],
                                      zhi[v % 2][:, 1:3, 0:k, :], ALU.subtract).then_inc(zlo_dve_ready, 1)

                def combine(q, v):
                    if v >= 2:
                        dve.wait_ge(mix2_done, KW * q + kws(v - 1))
                    n = count(v) * H
                    t = tcopy[v % 2][:, 0:n]
                    dve.wait_ge(t_copied, NU * q + v + 1)
                    dve.wait_ge(r_done, NU * q + v + 1)
                    dve.tensor_tensor(hid[v % 2][0:CB, 0, 0:n], t, ps[0:CB, R_BANK, 0:n],
                                      ALU.subtract).then_inc(mixed_ready, 1)
                    dve.wait_ge(mix1_done, NU * q + v + 1)
                    dve.tensor_tensor(hid[v % 2][0:CB, 1, 0:n], t, ps[0:CB, I_BANK, 0:n],
                                      ALU.add).then_inc(mixed_ready, 1)

                def shrink(q, v):
                    if v >= 2:
                        dve.wait_ge(shrunk, NU * q + v - 1)
                    pieces = [(0, 2), (2, 3)] if v == NU - 1 else [(0, count(v))]
                    for j, (a, b) in enumerate(pieces):
                        d, c = mixed2(v, a, b), clamped[v % 2][:, a:b, :]
                        if v:
                            lo = 2 * (kws(v) - 1)
                            dst = ydg[:, lo + 2 * a:lo + 2 * b, :].rearrange("p (k r) c -> p k (r c)", r=2)
                        else:
                            dst = edge[:].rearrange("p k r c -> p k (r c)")
                        dve.wait_ge(mix2_done, KW * q + kws(v) + b)
                        dve.tensor_scalar(c, d, LAMBD, -LAMBD, ALU.min, ALU.max).then_inc(clamp_done, 1)
                        dve.wait_ge(clamp_done, (NU + 1) * q + v + j + 1)
                        ins = dve.tensor_tensor(dst, d, c, ALU.subtract)
                    ins.then_inc(shrunk, 1)

                def finish(q, p, g):
                    a, b = odd_rows(g)
                    xm = mirror(xs[p], a, b)
                    u = ps[:, 2 * (g % 4), 0:HG * CB].rearrange("p (h c) -> p h c", c=CB)
                    dve.wait_ge(v_copied, NF * q + g + 1)
                    dve.tensor_tensor(xm, xm, vcopy[g % 3][:, 0:b - a, :], ALU.subtract).then_inc(minus_ready, 1)
                    xp = xs[p][:, HG * g:HG * g + HG, :]
                    dve.wait_ge(u_done, NF * q + g + 1)
                    dve.wait_ge(plus_ready, NF * q + g + 1)
                    dve.tensor_tensor(xp, u, xp, ALU.add)
                    dve.wait_ge(minus_ready, NF * q + g + 1)
                    dve.tensor_tensor(xm, u[:, a - HG * g:b - HG * g, :], xm, ALU.add).then_inc(y_ready, 1)

                dve.memset(hid[0][CB:CB + 1, 0, :], 1.0).then_inc(ones_set, 1)
                dve.memset(hid[1][CB:CB + 1, 0, :], 1.0).then_inc(ones_set, 1)
                dve.memset(clamped[0][0:1, 0, 0:1], 0.0).then_inc(y_ready, NF)
                dve.wait_ge(y_ready, NF)
                with dve.Fori(0, STEPS) as t:
                    for p in range(PAIRS):
                        q = t * PAIRS + p
                        lines(q, 0)
                        modes(q, 0)
                        modes(q, 1)
                        combine(q, 0)
                        modes(q, 2)
                        split_low(q, 2)
                        for v in range(LAG2, NU + LAG2):
                            if v < NU:
                                modes(q, v)
                            if v < NU + LAG1:
                                combine(q, v - LAG1)
                            shrink(q, v - LAG2)
                        lines(q, 1)
                        for g in range(NF):
                            finish(q, p, g)

            @block.gpsimd
            def _(pool):
                with pool.Fori(0, STEPS) as t:
                    pool.wait_ge(weights_loaded, (t + 1) * 16 * WEIGHT_DMAS)
                    pool.tensor_tensor(w1g[:, 1, :], w1g[:, 0, :], w1i[:], ALU.add)
                    pool.tensor_tensor(w1g[:, 2, :], w1i[:], w1g[:, 0, :], ALU.subtract).then_inc(w1g_ready, 1)
                    pool.wait_ge(w1hi_ready, t + 1)
                    pool.tensor_tensor(w1lo[:], w1g[:], w1hi[:], ALU.subtract).then_inc(w1lo_ready, 1)
                    for p in range(PAIRS):
                        q = t * PAIRS + p
                        for v in range(NU):
                            n = count(v)
                            zz, hi, lo = (t[v % 2] for t in (z, zhi, zlo))
                            pool.wait_ge(z_ready, NU * q + v + 1)
                            pool.tensor_tensor(zz[:, 0, 0:n, :], zz[:, 2, 0:n, :], zz[:, 1, 0:n, :],
                                               ALU.add).then_inc(zsum_ready, 1)
                            if v in WHOLE:
                                continue
                            if v - 2 in SPLIT:
                                pool.wait_ge(mix1_done, NU * q + v - 1)
                            if v not in DVE_SPLITS:
                                pool.wait_ge(zhi_ready, split_count(q, v))
                                pool.tensor_tensor(lo[:, 1:3, 0:n, :], zz[:, 1:3, 0:n, :], hi[:, 1:3, 0:n, :],
                                                   ALU.subtract).then_inc(zlo_ready, 1)
                            pool.wait_ge(zsum_hi_ready, split_count(q, v))
                            pool.tensor_tensor(lo[:, 0, 0:n, :], zz[:, 0, 0:n, :], hi[:, 0, 0:n, :],
                                               ALU.subtract).then_inc(zsum_lo_ready, 1)
                        for g in range(NF):
                            a, b = odd_rows(g)
                            xp = xs[p][:, a:b, :]
                            pool.wait_ge(v_copied, NF * q + g + 1)
                            pool.tensor_tensor(xp, xp, vcopy[g % 3][:, 0:b - a, :], ALU.add).then_inc(plus_ready, 1)


def kernel(x, L0_conv_w1, L0_conv_b1, L0_conv_w2, L0_conv_b2):
    import numpy as np
    import concourse.bacc as bacc
    from concourse.bass_utils import run_bass_kernel_spmd

    nc = bacc.Bacc("TRN2", target_bir_lowering=False, num_devices=1)
    arrays = {"x": x, "w1": L0_conv_w1, "b1": L0_conv_b1, "w2": L0_conv_w2, "b2": L0_conv_b2,
              "table": transform_table()}
    arrays = {name: np.ascontiguousarray(a) for name, a in arrays.items()}
    args = [nc.dram_tensor(f"in_{name}", a.shape, mybir.dt.from_np(a.dtype), kind="ExternalInput").ap()
            for name, a in arrays.items()]
    out = nc.dram_tensor("out", (B, H, W, C), F32, kind="ExternalOutput").ap()
    build(nc, *args, out)
    r = run_bass_kernel_spmd(nc, [{f"in_{name}": a for name, a in arrays.items()}], core_ids=[0])
    return r.results[0]["out"]
```
